# Optimizing a Trainium2 kernel written in Bass

```python
import numpy as np
import jax
import jax.numpy as jnp

def _softmax(x, axis=-1):
    return jax.nn.softmax(x, axis=axis)

def _gelu(x):
    return jax.nn.gelu(x, approximate=True)

def _silu(x):
    return jax.nn.silu(x)

def _sigmoid(x):
    return jax.nn.sigmoid(x)

def _layernorm(x, axis=-1, eps=1e-05):
    m = jnp.mean(x, axis=axis, keepdims=True)
    v = jnp.var(x, axis=axis, keepdims=True)
    return (x - m) / jnp.sqrt(v + eps)

def _scatter_add(tgt, idx, src, axis=0):
    return tgt.at[idx].add(src)

def _segment_sum(src, seg, n):
    return jax.ops.segment_sum(src, seg, n)
kernel_name = 'mk_gnn_resnorm_d2_gnn_r8_c8f825'

def setup_inputs(seed: int=0):
    np.random.seed(seed)
    _w = jnp.asarray

    def _rec_inputs():
        import jax
        import jax.numpy as jnp
        _gk = jax.random.key(seed)
        x = 0.0002685 + 0.9999 * jax.random.normal(jax.random.fold_in(_gk, 1), (6250, 256), jnp.float32)
        _s = jax.random.randint(jax.random.fold_in(_gk, 2), (50000,), 0, 6250, jnp.int32)
        _d = jax.random.randint(jax.random.fold_in(_gk, 3), (50000,), 0, 6250, jnp.int32)
        _loop = jnp.arange(6250, dtype=jnp.int32)
        src = jnp.concatenate([_s, _d, _loop])
        dst = jnp.concatenate([_d, _s, _loop])
        _o = jnp.argsort(dst, stable=True)
        src = src[_o]
        dst = dst[_o]
        edge_type_8 = jax.random.randint(jax.random.fold_in(_gk, 12), (106250,), 0, 8, jnp.int32)
        return (x, src, dst, edge_type_8)
    x, src, dst, edge_type_8 = _rec_inputs()

    def _L0_gnn_setup():
        import jax, jax.numpy as jnp
        import numpy as np
        NUM_NODES = 5000
        NUM_REL = 8
        NUM_BASES = 4
        EMB = 256
        NUM_LAYERS = 3
        NUM_EDGES = 80000

        def _rgcn_layer(x, src, seg, inv_cnt, comp, basis, root, bias):
            N, D = x.shape
            R = comp.shape[0]
            W = jnp.einsum('rb,bio->rio', comp, basis)
            agg = jax.ops.segment_sum(x[src], seg, num_segments=R * N) * inv_cnt
            agg = agg.reshape(R, N, D)
            out = jnp.einsum('rni,rio->no', agg, W) + x @ root + bias
            return out
        key = jax.random.key(seed)
        ks = jax.random.split(key, 7)
        edge_index = jax.random.randint(ks[0], (2, NUM_EDGES), 0, NUM_NODES)
        edge_type = jax.random.randint(ks[1], (NUM_EDGES,), 0, NUM_REL)
        embeddings = jax.random.normal(ks[2], (NUM_NODES, EMB), dtype=jnp.float32)
        scale = 1.0 / np.sqrt(EMB)
        comps = jax.random.normal(ks[3], (NUM_LAYERS, NUM_REL, NUM_BASES), dtype=jnp.float32) * scale
        bases = jax.random.normal(ks[4], (NUM_LAYERS, NUM_BASES, EMB, EMB), dtype=jnp.float32) * scale
        roots = jax.random.normal(ks[5], (NUM_LAYERS, EMB, EMB), dtype=jnp.float32) * scale
        biases = jnp.zeros((NUM_LAYERS, EMB), dtype=jnp.float32)
        return {'edge_index': edge_index, 'edge_type': edge_type, 'embeddings': embeddings, 'comps': comps, 'bases': bases, 'roots': roots, 'biases': biases}
    _L0_gnn_all = _L0_gnn_setup()
    _L0_gnn_in = {k: v for k, v in _L0_gnn_all.items() if k in ('comps', 'bases', 'roots', 'biases')}
    del _L0_gnn_all

    def _L1_gnn_setup():
        import jax, jax.numpy as jnp
        import numpy as np
        N = 6250
        E = 100000
        IN_C = 256
        HEADS = 8
        OUT_C = 32
        key = jax.random.key(seed)
        k1, k2, k3, k4, k5 = jax.random.split(key, 5)
        x = jax.random.normal(k1, (N, IN_C), dtype=jnp.float32)
        edge_index = jax.random.randint(k2, (2, E), 0, N, dtype=jnp.int64)
        lim_W = float(np.sqrt(6.0 / (IN_C + HEADS * OUT_C)))
        lim_a = float(np.sqrt(6.0 / (HEADS + OUT_C)))
        W = jax.random.uniform(k3, (IN_C, HEADS * OUT_C), minval=-lim_W, maxval=lim_W, dtype=jnp.float32)
        a_src = jax.random.uniform(k4, (HEADS, OUT_C), minval=-lim_a, maxval=lim_a, dtype=jnp.float32)
        a_dst = jax.random.uniform(k5, (HEADS, OUT_C), minval=-lim_a, maxval=lim_a, dtype=jnp.float32)
        return {'x': x, 'edge_index': edge_index, 'W': W, 'a_src': a_src, 'a_dst': a_dst}
    _L1_gnn_all = _L1_gnn_setup()
    _L1_gnn_in = {k: v for k, v in _L1_gnn_all.items() if k in ('W', 'a_src', 'a_dst')}
    del _L1_gnn_all
    return {'x': x, 'src': src, 'dst': dst, 'edge_type_8': edge_type_8, 'L0_gnn_comps': _L0_gnn_in['comps'], 'L0_gnn_bases': _L0_gnn_in['bases'], 'L0_gnn_roots': _L0_gnn_in['roots'], 'L0_gnn_biases': _L0_gnn_in['biases'], 'L1_gnn_W': _L1_gnn_in['W'], 'L1_gnn_a_src': _L1_gnn_in['a_src'], 'L1_gnn_a_dst': _L1_gnn_in['a_dst']}

def reference(x, src, dst, edge_type_8, L0_gnn_comps, L0_gnn_bases, L0_gnn_roots, L0_gnn_biases, L1_gnn_W, L1_gnn_a_src, L1_gnn_a_dst):
    import jax
    import jax.numpy as jnp

    def _L0_gnn_ref(edge_index, edge_type, embeddings, comps, bases, roots, biases):
        import jax, jax.numpy as jnp
        import numpy as np
        NUM_NODES = 5000
        NUM_REL = 8
        NUM_BASES = 4
        EMB = 256
        NUM_LAYERS = 3
        NUM_EDGES = 80000

        def _rgcn_layer(x, src, seg, inv_cnt, comp, basis, root, bias):
            N, D = x.shape
            R = comp.shape[0]
            W = jnp.einsum('rb,bio->rio', comp, basis)
            agg = jax.ops.segment_sum(x[src], seg, num_segments=R * N) * inv_cnt
            agg = agg.reshape(R, N, D)
            out = jnp.einsum('rni,rio->no', agg, W) + x @ root + bias
            return out
        src, dst = (edge_index[0], edge_index[1])
        N = embeddings.shape[0]
        R = comps.shape[1]
        seg = edge_type * N + dst
        cnt = jax.ops.segment_sum(jnp.ones_like(seg, dtype=embeddings.dtype), seg, num_segments=R * N)
        inv_cnt = (1.0 / jnp.maximum(cnt, 1.0))[:, None]
        x = _rgcn_layer(embeddings, src, seg, inv_cnt, comps[0], bases[0], roots[0], biases[0])
        for i in range(1, NUM_LAYERS - 1):
            x = _rgcn_layer(jax.nn.relu(x), src, seg, inv_cnt, comps[i], bases[i], roots[i], biases[i])
        return x

    def _L1_gnn_ref(x, edge_index, W, a_src, a_dst):
        import jax, jax.numpy as jnp
        import numpy as np
        N = 6250
        E = 100000
        IN_C = 256
        HEADS = 8
        OUT_C = 32
        n = x.shape[0]
        H, D = a_src.shape
        x_proj = (x @ W).reshape(n, H, D)
        alpha_src = jnp.einsum('nhd,hd->nh', x_proj, a_src)
        alpha_dst = jnp.einsum('nhd,hd->nh', x_proj, a_dst)
        row, col = (edge_index[0], edge_index[1])
        e = alpha_src[row] + alpha_dst[col]
        m = jax.ops.segment_max(e, col, num_segments=n)
        m = jnp.where(jnp.isfinite(m), m, 0.0)
        e_exp = jnp.exp(e - m[col])
        s = jax.ops.segment_sum(e_exp, col, num_segments=n)
        att = e_exp / (s[col] + 1e-16)
        out = jax.ops.segment_sum(att[:, :, None] * x_proj[row], col, num_segments=n)
        return out.reshape(n, H * D)
    edge_index = jnp.stack([src, dst])
    x = _layernorm(x + _L0_gnn_ref(edge_index, edge_type_8, x, L0_gnn_comps, L0_gnn_bases, L0_gnn_roots, L0_gnn_biases), axis=-1)
    x = _layernorm(x + _L1_gnn_ref(x, edge_index, L1_gnn_W, L1_gnn_a_src, L1_gnn_a_dst), axis=-1)
    return x

_drawn_inputs = setup_inputs


def setup_inputs(seed=0):
    import zlib

    import numpy as np

    out = dict(_drawn_inputs(seed))
    spreads = {'L0_gnn_biases': (0.0, 0.1)}
    factors = {}
    for name, (base, spread) in spreads.items():
        noise = np.random.default_rng([zlib.crc32(name.encode()), seed]).standard_normal(out[name].shape)
        drawn = base * np.exp(spread * noise) if base else spread * noise
        out[name] = jnp.asarray(drawn.astype(out[name].dtype))
    for name, factor in factors.items():
        out[name] = (out[name] * factor).astype(out[name].dtype)
    return out
```

```python
import numpy as np

import concourse.bass as bass
from concourse import mybir
from contextlib import ExitStack

F32 = mybir.dt.float32
I32 = mybir.dt.int32
U32 = mybir.dt.uint32
U8 = mybir.dt.uint8
ALU = mybir.AluOpType
ACT = mybir.ActivationFunctionType
AX = mybir.AxisListType

P = 128
N, D, E = 6250, 256, 106250
R, NB = 8, 4
HD, OC = 8, 32
TILES = -(-N // P)
NP = TILES * P
LAST = N - (TILES - 1) * P
BLOCKS = 16
BCH = 52
BE = BCH * P
CHUNKS = BLOCKS * BCH
CG = -(-CHUNKS // P)
SG = 7
STEPS = SG * P
BS = 8
RG_BATCHES = 110
GAT_BATCHES = 111
GRP = 7
AW = OC + 1
GW = HD * AW
XW = GW + HD
BIG = 1.0e30
PAD_DST = 8191.0
EPS = 1e-5
FULL_CH = E // P
TAIL = E - FULL_CH * P
assert CHUNKS >= -(-E // P) and RG_BATCHES * BS >= -(-E // P) + TILES - 1 and GRP * 7 == TILES
assert (GAT_BATCHES + 1) * BS == STEPS and CHUNKS < CG * P


def flat_ap(ap, offset, dims):
    return bass.AP(ap.tensor, offset, dims)


class Kit:

    def __init__(self, nc):
        self.nc = nc
        self.n = 0

    def sb(self, ctx, name, shape, dt=F32):
        return ctx.enter_context(self.nc.sbuf_tensor(name, shape, dt))

    def ps(self, ctx, name, cols=512):
        return ctx.enter_context(self.nc.psum_tensor(name, [P, cols], F32))

    def sem(self, ctx, name):
        return ctx.enter_context(self.nc.semaphore(name))


def chain(eng, sem):
    count = [0]

    def link(ins):
        count[0] += 1
        ins.then_inc(sem, 1)
        eng.wait_ge(sem, count[0])
    return link


def pe_transpose_tile(nc, pe, j, i, b):
    b.wait_src(pe, j, i)
    for k in range(2):
        ins = nc.tensor.transpose(b.psT[:, k * P:(k + 1) * P], b.src[:, i, k * P:(k + 1) * P], b.ident[:, :])
    ins.then_inc(b.hT_ps, 1)


def pe_transform_tile(nc, pe, j, i, last, b):
    t = j * GRP + i
    pe.wait_ge(b.hT_sb, t + 1)
    if not last:
        pe_transpose_tile(nc, pe, j + (i + 1) // GRP, (i + 1) % GRP, b)
    for q in range(5):
        pe.wait_ge(b.evac, t * 5 + q + 1)
        w = 512 if q < 4 else D
        for k in range(2):
            rhs = b.W[:, k, q * 512:(q + 1) * 512] if q < 4 else b.root[:, k, :]
            ins = nc.tensor.matmul(b.psY[q][:, 0:w], b.hT[:, i, k * P:(k + 1) * P], rhs, start=(k == 0), stop=(k == 1 and q < 4))
        if q == 4:
            ins = nc.tensor.matmul(b.psY[q][:, 0:w], b.ones[0:1, :], b.bias[0:1, :], start=False, stop=True)
        ins.then_inc(b.mm, 1)


def act_transposed(nc, act, j, i, b):
    act.wait_ge(b.hT_ps, j * GRP + i + 1)
    nc.scalar.activation(b.hT[:, i, :], b.psT[:, 0:D], ACT.Copy).then_inc(b.hT_sb, 1)


def act_transform_tile(nc, act, j, i, first, last, b):
    t = j * GRP + i
    if not last:
        act_transposed(nc, act, j + (i + 1) // GRP, (i + 1) % GRP, b)
    b.refill(act, j, i)
    view = b.y_tab.rearrange("(r n) c -> n r c", n=NP)
    for q in range(5):
        act.wait_ge(b.mm, t * 5 + q + 1)
        if q == 4:
            act.sem_inc(b.act_go, 1)
            nc.scalar.activation(b.acc[:, bass.ds(t * D, D)], b.psY[q][:, 0:D], ACT.Copy).then_inc(b.evac, 1)
            continue
        half = q // 2
        if q % 2 == 0 and not first:
            act.wait_ge(b.stored[half], t * 16)
        nc.scalar.activation(b.Y[:, q, :], b.psY[q][:, :], ACT.Copy).then_inc(b.evac, 1)
        if q % 2:
            act.wait_ge(b.evac, CREDIT_EVAC + t * 5 + q + 1)
            act.dma_start(view[bass.ds(t * P, P), half * 4:half * 4 + 4, :],
                          b.Y[:, 2 * half:2 * half + 2, :].rearrange("p q (r c) -> p (q r) c", c=D)).then_inc(b.stored[half], 16)


def act_transform(nc, act, b):
    act.sem_inc(b.evac, CREDIT_EVAC)
    act_transposed(nc, act, 0, 0, b)
    for i in range(GRP):
        act_transform_tile(nc, act, 0, i, i == 0, False, b)
    with act.Fori(1, GRP - 2) as j:
        for i in range(GRP):
            act_transform_tile(nc, act, j, i, False, False, b)
    for j in (GRP - 2, GRP - 1):
        for i in range(GRP):
            act_transform_tile(nc, act, j, i, False, (j, i) == (GRP - 1, GRP - 1), b)
    for half in range(2):
        act.wait_ge(b.stored[half], 16 * TILES)


CREDIT_EVAC = 5


class Bag:
    pass


def build(nc, x, src, dst, typ, comps, bases, roots, biases, gat_w, gat_as, gat_ad, out):
    kit = Kit(nc)
    edge_tab = nc.dram_tensor("edge_tab", (CHUNKS, 4 * P), F32).ap()
    y_tab = nc.dram_tensor("y_tab", (R * NP, D), F32).ap()
    h_tab = nc.dram_tensor("h_tab", (NP, D), F32).ap()
    xp_tab = nc.dram_tensor("xp_tab", (NP, XW), F32).ap()
    key_tab = nc.dram_tensor("key_tab", (1, 1 + STEPS * P), F32).ap()
    pen_tab = nc.dram_tensor("pen_tab", (1, STEPS * P), F32).ap()
    tile_tab = nc.dram_tensor("tile_tab", (STEPS, 1), I32).ap()

    with ExitStack() as top:
        ident = kit.sb(top, "ident", [P, P])
        ones = kit.sb(top, "ones", [P, P])
        iota = kit.sb(top, "iota", [P, P])
        step_tab = kit.sb(top, "step_tab", [P, STEPS, 2])
        yrow = kit.sb(top, "yrow", [P, STEPS], U32)
        srow = kit.sb(top, "srow", [P, STEPS], U32)
        tile_row = kit.sb(top, "tile_row", [1, BS + STEPS], I32)

        adst = kit.sb(top, "adst", [P, TILES * HD])
        with ExitStack() as mid:
            acc = kit.sb(mid, "acc", [P, TILES * D])
            prepare_and_transform(nc, kit, x, src, dst, typ, comps, bases, roots, biases, ident, ones, iota,
                                  step_tab, yrow, srow, tile_row, acc, edge_tab, y_tab, key_tab, tile_tab)
            rgcn_gather(nc, kit, "a", iota, step_tab, yrow, tile_row, acc, y_tab)
            second_transform(nc, kit, comps, bases, roots, biases, ident, ones, acc, y_tab, key_tab, pen_tab)
            rgcn_gather(nc, kit, "b", iota, step_tab, yrow, tile_row, acc, y_tab)
            project(nc, kit, x, gat_w, gat_as, gat_ad, ident, acc, adst, h_tab, xp_tab)
        with ExitStack() as mid:
            acc = kit.sb(mid, "acc_gat", [P, TILES * GW])
            gat_gather(nc, kit, ident, ones, iota, step_tab, srow, tile_row, acc, adst, xp_tab, pen_tab)
            finish(nc, kit, acc, h_tab, out)


def load_weights(nc, eng, sem, comps, bases, roots, biases, layer, B, comp, root, bias):
    eng.dma_start(B[:, :, :, :], bases[layer, :, :, :].rearrange("b (k p) o -> p b k o", p=P)).then_inc(sem, 16)
    eng.dma_start(comp[:, :], flat_ap(comps, layer * R * NB, [[0, P], [1, R * NB]])).then_inc(sem, 16)
    eng.dma_start(root[:, :, :], roots[layer, :, :].rearrange("(k p) o -> p k o", p=P)).then_inc(sem, 16)
    eng.dma_start(bias[:, :], biases[layer:layer + 1, :]).then_inc(sem, 16)


def mix_bases(nc, link, W, B, comp):
    Wv = W[:, :, :].rearrange("p k (r o) -> p k r o", o=D)
    for r in range(R):
        link(nc.vector.tensor_scalar(Wv[:, :, r, :], B[:, 0, :, :], comp[:, r * NB:r * NB + 1], None, ALU.mult))
        for c in range(1, NB):
            link(nc.vector.scalar_tensor_tensor(out=Wv[:, :, r, :], in0=B[:, c, :, :], scalar=comp[:, r * NB + c:r * NB + c + 1],
                                                in1=Wv[:, :, r, :], op0=ALU.mult, op1=ALU.add))


def prepare_and_transform(nc, kit, x, src, dst, typ, comps, bases, roots, biases, ident, ones, iota,
                          step_tab, yrow, srow, tile_row, acc, edge_tab, y_tab, key_tab, tile_tab):
    with ExitStack() as ctx:
        def sb(name, shape, dt=F32):
            return kit.sb(ctx, "p_" + name, shape, dt)

        def sem(name):
            return kit.sem(ctx, "p_" + name)

        b = Bag()
        b.W = sb("W", [P, 2, R * D])
        b.root = sb("root", [P, 2, D])
        b.bias = sb("bias", [1, D])
        b.src = sb("xin", [P, GRP, D])
        b.hT = sb("hT", [P, GRP, D])
        b.Y = sb("Y", [P, 4, 512])
        b.ident, b.ones, b.acc = ident, ones, acc
        basis = sb("basis", [P, NB, 2, D])
        comp = sb("comp", [P, R * NB])
        dblk = sb("dblk", [P, BE + 2], I32)
        tblk = sb("tblk", [P, BE], I32)
        same = sb("same", [P, BE + 4], U8)
        hit = sb("hit", [P, BE], U8)
        ech = sb("ech", [P, 3, CG, P], I32)
        echf = sb("echf", [P, CG, 3, P])
        chlast = hit[:, 0:CG * (TILES - 1) * 4].bitcast(F32).rearrange("p (g t) -> p g t", g=CG)
        tfirst = sb("tfirst", [P, TILES - 1])
        tnum = sb("tnum", [P, TILES - 1])
        tstart = same[:, 0:(TILES - 1) * 4].bitcast(F32)
        cmp_junk = same[:, 256:256 + (TILES - 1) * 4].bitcast(F32)
        snum = sb("snum", [P, SG])
        ts = sb("ts", [P, SG])
        ts128 = sb("ts128", [P, SG])
        tsi = sb("tsi", [P, SG], I32)
        cs = sb("cs", [P, SG])
        csi = sb("csi", [P, SG], U32)
        relr = ech[:, 0, :, :].bitcast(F32)
        pidx = sb("pidx", [P, 1], I32)
        pdiv = sb("pdiv", [P, 2], I32)
        rnum = sb("rnum", [P, 1])
        kmod = sb("kmod", [P, 1])
        ksel = sb("ksel", [P, BLOCKS])
        ends = sb("ends", [P, 4])
        spent = basis[0:1, :, :, :].rearrange("p b k o -> p (b k o)")
        endrow, trow, inirow = (spent[:, a * P:z * P].rearrange("o (f p) -> o f p", p=P) for a, z in ((0, 4), (4, 6), (6, 8)))
        ini = sb("ini", [P, 2])
        neg1 = sb("neg1", [1, 1])
        pre = tblk[:, :].bitcast(F32)
        suf = dblk[:, 0:BE].bitcast(F32)
        wrow = dblk[0:BLOCKS, 0:BE].bitcast(F32)
        srt = tblk[:, 0:SG * 4 * P].bitcast(F32).rearrange("p (g f) -> p g f", g=SG)

        b.psY = [kit.ps(ctx, f"p_psY{q}") for q in range(5)]
        b.psT = kit.ps(ctx, "p_psT")
        psA = kit.ps(ctx, "p_psA")
        psB = kit.ps(ctx, "p_psB")

        b.y_tab = y_tab
        b.act_go, b.hT_ps, b.hT_sb, b.mm, b.evac = sem("act_go"), sem("hT_ps"), sem("hT_sb"), sem("mm"), sem("evac")
        b.stored = [sem("stored0"), sem("stored1")]
        x_in = [sem(f"x_in{i}") for i in range(GRP)]

        def wait_src(pe, j, i):
            pe.wait_ge(x_in[i], (j + 1) * 16)

        def refill(act, j, i):
            if isinstance(j, int) and j == GRP - 1:
                return
            n = (j + 1) * GRP + i
            rows = LAST if isinstance(n, int) and n == TILES - 1 else P
            act.dma_start(b.src[0:rows, i, :], x[bass.ds(n * P, rows), :]).then_inc(x_in[i], 16)
        b.wait_src, b.refill = wait_src, refill
        w_in, edges_in, blk_in = sem("w_in"), sem("edges_in"), sem("blk_in")
        padded, w_ready, consts, dve = sem("padded"), sem("w_ready"), sem("consts"), sem("dve")
        tab_ready, cmp_ready, cnt_ps, cs_ready = sem("tab_ready"), sem("cmp_ready"), sem("cnt_ps"), sem("cs_ready")
        tab_out, ends_ready, ends_ps, ini_ready, ini_ps = sem("tab_out"), sem("ends_ready"), sem("ends_ps"), sem("ini_ready"), sem("ini_ps")
        own_ready, own_ps, own_free, wrow_ready = sem("own_ready"), sem("own_ps"), sem("own_free"), sem("wrow_ready")
        rows_in, rel_ready, col_ps, col_free = sem("rows_in"), sem("rel_ready"), sem("col_ps"), sem("col_free")
        out_sem, tile_in, const_chain = sem("out_sem"), sem("tile_in"), sem("const_chain")

        with nc.Block() as block:
            @block.gpsimd
            def _(pool):
                link = chain(pool, const_chain)
                for t, v in ((ident, 0.0), (ones, 1.0), (neg1, -1.0)):
                    link(nc.gpsimd.memset(t[:, :], v))
                link(nc.gpsimd.affine_select(out=ident[:, :], in_=ident[:, :], compare_op=ALU.not_equal, fill=1.0, base=0,
                                             pattern=[[-1, P]], channel_multiplier=1))
                link(nc.gpsimd.iota(iota[:, :], pattern=[[1, P]], base=0, channel_multiplier=0, allow_small_or_imprecise_dtypes=True))
                link(nc.gpsimd.iota(tfirst[:, :], pattern=[[P, TILES - 1]], base=P, channel_multiplier=0, allow_small_or_imprecise_dtypes=True))
                link(nc.gpsimd.iota(tnum[:, :], pattern=[[1, TILES - 1]], base=1, channel_multiplier=0, allow_small_or_imprecise_dtypes=True))
                link(nc.gpsimd.iota(snum[:, :], pattern=[[P, SG]], base=0, channel_multiplier=1, allow_small_or_imprecise_dtypes=True))
                nc.gpsimd.iota(pidx[:, :], pattern=[[0, 1]], base=0, channel_multiplier=1).then_inc(consts, 1)
                pool.wait_ge(tab_out, 16 * 3)
                pool.wait_ge(cs_ready, 1)
                for g in range(SG):
                    nc.gpsimd.indirect_dma_start(srt[:, g, :], None, edge_tab, bass.IndirectOffsetOnAxis(ap=csi[:, g:g + 1], axis=0)).then_inc(rows_in, 16)

            @block.sync
            def _(sp):
                load_weights(nc, sp, w_in, comps, bases, roots, biases, 0, basis, comp, b.root, b.bias)
                for t in range(GRP):
                    sp.dma_start(b.src[:, t, :], x[t * P:(t + 1) * P, :]).then_inc(x_in[t], 16)
                sp.wait_ge(padded, 1)
                for f, a in enumerate((dst, typ, src)):
                    main = (CG - 1) * P * P
                    rest = FULL_CH - (CG - 1) * P
                    sp.dma_start(ech[:, f, 0:CG - 1, :], a[0:main].rearrange("(g p e) -> p g e", p=P, e=P)).then_inc(edges_in, 16)
                    sp.dma_start(ech[0:rest, f, CG - 1, :], a[main:FULL_CH * P].rearrange("(p e) -> p e", e=P)).then_inc(edges_in, 16)
                    sp.dma_start(ech[rest:rest + 1, f, CG - 1, 0:TAIL], a[FULL_CH * P:E].rearrange("(p e) -> p e", p=1)).then_inc(edges_in, 16)
                for r in range(R):
                    o, last = r * BLOCKS, (BLOCKS - 1) * BE
                    sp.dma_start(dblk[o:o + 1, 1:BE + 2], flat_ap(dst, 0, [[BE, 1], [1, BE + 1]])).then_inc(blk_in, 16)
                    sp.dma_start(dblk[o + 1:o + BLOCKS - 1, :], flat_ap(dst, BE - 1, [[BE, BLOCKS - 2], [1, BE + 2]])).then_inc(blk_in, 16)
                    sp.dma_start(dblk[o + BLOCKS - 1:o + BLOCKS, 0:E - last + 1], flat_ap(dst, last - 1, [[BE, 1], [1, E - last + 1]])).then_inc(blk_in, 16)
                    sp.dma_start(tblk[o:o + BLOCKS - 1, :], flat_ap(typ, 0, [[BE, BLOCKS - 1], [1, BE]])).then_inc(blk_in, 16)
                    sp.dma_start(tblk[o + BLOCKS - 1:o + BLOCKS, 0:E - last], flat_ap(typ, last, [[BE, 1], [1, E - last]])).then_inc(blk_in, 16)
                sp.wait_ge(tab_ready, 1)
                view = edge_tab[0:(CG - 1) * P, :].rearrange("(g p) f -> p g f", p=P)
                sp.dma_start(view[:, :, 0:3 * P], echf[:, 0:CG - 1, :, :].rearrange("p g f e -> p g (f e)")).then_inc(tab_out, 16)
                sp.dma_start(edge_tab[(CG - 1) * P:CHUNKS, 0:3 * P], echf[0:CHUNKS - (CG - 1) * P, CG - 1, :, :].rearrange("p f e -> p (f e)")).then_inc(tab_out, 16)
                with nc.allow_non_contiguous_dma(reason="one tile number a step"):
                    sp.wait_ge(cs_ready, 1)
                    sp.dma_start(tile_tab.rearrange("(g p) o -> p (g o)", p=P), tsi[:, :]).then_inc(out_sem, 16)
                sp.dma_start(key_tab[0:1, 0:1], neg1[:, :]).then_inc(out_sem, 16)
                sp.wait_ge(out_sem, 32)
                sp.dma_start(tile_row[0:1, BS:BS + STEPS], tile_tab.rearrange("(o s) i -> o (s i)", o=1)).then_inc(tile_in, 16)
                sp.wait_ge(wrow_ready, 1)
                sp.dma_start(edge_tab[:, 3 * P:4 * P].rearrange("(k m) e -> k m e", k=BLOCKS), wrow.rearrange("k (m e) -> k m e", e=P)).then_inc(tab_out, 16)
                sp.wait_ge(rows_in, 16 * SG)
                sp.dma_start(flat_ap(key_tab, 1, [[P, P], [P * P, SG], [1, P]]), srt[:, :, 0:P]).then_inc(out_sem, 16)
                sp.wait_ge(out_sem, 48)
                sp.wait_ge(tile_in, 16)
            @block.vector
            def _(dve_e):
                link = chain(dve_e, dve)
                v = nc.vector
                link(v.memset(tile_row[:, :], 0))
                link(v.memset(ech[:, 0, CG - 1, :], int(PAD_DST)))
                link(v.memset(ech[:, 1:3, CG - 1, :], 0))
                link(v.memset(dblk[:, 0:1], -1))
                link(v.memset(dblk[:, E - (BLOCKS - 1) * BE + 1:BE + 2], int(PAD_DST)))
                v.memset(tblk[:, E - (BLOCKS - 1) * BE:BE], 0).then_inc(padded, 1)
                dve_e.wait_ge(w_in, 64)
                mix_bases(nc, link, b.W, basis, comp)
                v.memset(inirow[:, :, :], 0.0).then_inc(w_ready, 1)
                dve_e.wait_ge(edges_in, 16 * 9)
                dve_e.wait_ge(consts, 1)
                link(v.tensor_copy(echf[:, :, 0, :], ech[:, 0, :, :]))
                link(v.tensor_copy(echf[:, :, 2, :], ech[:, 2, :, :]))
                v.scalar_tensor_tensor(out=echf[:, :, 1, :], in0=ech[:, 1, :, :], scalar=float(NP), in1=ech[:, 2, :, :],
                                       op0=ALU.mult, op1=ALU.add).then_inc(tab_ready, 1)
                for g in range(CG):
                    ins = v.tensor_scalar(chlast[:, g, :], tfirst[:, :], echf[:, g, 0, P - 1:P], None, ALU.is_gt)
                ins.then_inc(cmp_ready, 1)
                dve_e.wait_ge(cnt_ps, 1)
                link(v.tensor_tensor(tstart[:, :], tnum[:, :], psA[:, 0:TILES - 1], ALU.add))
                for g in range(SG):
                    link(v.tensor_scalar(cmp_junk[:, :], tstart[:, :], snum[:, g:g + 1], None, ALU.is_le, ALU.add, accum_out=ts[:, g:g + 1]))
                link(v.tensor_scalar(ts128[:, :], ts[:, :], float(P), None, ALU.mult))
                link(v.tensor_copy(tsi[:, :], ts[:, :]))
                link(v.tensor_tensor(cs[:, :], snum[:, :], ts[:, :], ALU.subtract))
                link(v.tensor_scalar(cs[:, :], cs[:, :], float(CHUNKS - 1), None, ALU.min))
                v.tensor_copy(csi[:, :], cs[:, :]).then_inc(cs_ready, 1)
                link(v.tensor_scalar(pdiv[:, 0:1], pidx[:, :], 4, None, ALU.arith_shift_right))
                link(v.tensor_scalar(pdiv[:, 1:2], pidx[:, :], BLOCKS - 1, None, ALU.bitwise_and))
                link(v.tensor_copy(rnum[:, :], pdiv[:, 0:1]))
                link(v.tensor_copy(kmod[:, :], pdiv[:, 1:2]))
                link(v.tensor_scalar(ksel[:, :], iota[:, 0:BLOCKS], kmod[:, :], None, ALU.is_equal))
                dve_e.wait_ge(blk_in, 16 * 5 * R)
                link(v.tensor_tensor(same[:, 0:BE + 1], dblk[:, 0:BE + 1], dblk[:, 1:BE + 2], ALU.is_equal))
                link(v.tensor_scalar(hit[:, :], tblk[:, :], rnum[:, :], None, ALU.is_equal))
                link(v.tensor_tensor(ends[:, 1:2], dblk[:, 0:1], dblk[:, BE:BE + 1], ALU.is_equal))
                link(v.tensor_tensor(ends[:, 3:4], dblk[:, 1:2], dblk[:, BE + 1:BE + 2], ALU.is_equal))

                def scans(left, right):
                    link(v.tensor_tensor_scan(pre[:, :], same[:, 0:BE], hit[:, :], left, ALU.mult, ALU.add))
                    link(v.tensor_tensor_scan(suf[:, ::-1], same[:, 1:BE + 1][:, ::-1], hit[:, ::-1], right, ALU.mult, ALU.add))

                scans(0.0, 0.0)
                link(v.tensor_copy(ends[:, 0:1], pre[:, BE - 1:BE]))
                v.tensor_copy(ends[:, 2:3], suf[:, 0:1]).then_inc(ends_ready, 1)
                dve_e.wait_ge(ends_ps, 1)
                link(v.tensor_copy(endrow[:, :, :].rearrange("o f p -> o (f p)"), psB[0:1, :]))
                link(v.tensor_tensor_scan(trow[:, 0, :], endrow[:, 1, :], endrow[:, 0, :], 0.0, ALU.mult, ALU.add))
                link(v.tensor_tensor_scan(trow[:, 1, ::-1], endrow[:, 3, ::-1], endrow[:, 2, ::-1], 0.0, ALU.mult, ALU.add))
                link(v.tensor_copy(inirow[:, 0, 1:P], trow[:, 0, 0:P - 1]))
                v.tensor_copy(inirow[:, 1, 0:P - 1], trow[:, 1, 1:P]).then_inc(ini_ready, 1)
                dve_e.wait_ge(ini_ps, 1)
                link(v.tensor_copy(ini[:, :], psA[:, 64:66]))
                scans(ini[:, 0:1], ini[:, 1:2])
                link(v.scalar_tensor_tensor(out=pre[:, :], in0=pre[:, :], scalar=-1.0, in1=suf[:, :], op0=ALU.add, op1=ALU.add))
                v.tensor_tensor(pre[:, :], pre[:, :], hit[:, :], ALU.mult).then_inc(own_ready, 1)
                for q in range(BE // 512):
                    dve_e.wait_ge(own_ps, q + 1)
                    ins = v.reciprocal(wrow[:, q * 512:(q + 1) * 512], (psA if q % 2 else psB)[0:BLOCKS, :])
                    ins.then_inc(own_free, 1)
                dve_e.wait_ge(own_free, BE // 512)
                v.memset(cmp_junk[:, :], 0.0).then_inc(wrow_ready, 1)
                dve_e.wait_ge(rows_in, 16 * SG)
                for g in range(SG):
                    ins = v.tensor_scalar(relr[:, g, :], srt[:, g, 0:P], ts128[:, g:g + 1], None, ALU.subtract)
                ins.then_inc(rel_ready, 1)
                n = 0
                for g in range(SG):
                    for f in range(4):
                        dve_e.wait_ge(col_ps, n + 1)
                        o = (psA if n % 2 else psB)[:, 0:P]
                        cols = slice(g * P, (g + 1) * P)
                        to = (step_tab[:, cols, 0], yrow[:, cols], srow[:, cols], step_tab[:, cols, 1])[f]
                        v.tensor_copy(to, o).then_inc(col_free, 1)
                        n += 1

            @block.scalar
            def _(act):
                act_transform(nc, act, b)

            @block.tensor
            def _(pe):
                pe.wait_ge(w_ready, 1)
                pe.wait_ge(consts, 1)
                pe.wait_ge(cmp_ready, 1)
                for g in range(CG):
                    ins = nc.tensor.matmul(psA[:, 0:TILES - 1], ones[:, :], chlast[:, g, :], start=(g == 0), stop=(g == CG - 1))
                ins.then_inc(cnt_ps, 1)

                def counts():
                    pe.wait_ge(ends_ready, 1)
                    for f in range(4):
                        ins = nc.tensor.matmul(psB[0:1, f * P:(f + 1) * P], ends[:, f:f + 1], ident[:, :], start=True, stop=True)
                    ins.then_inc(ends_ps, 1)
                    pe.wait_ge(ini_ready, 1)
                    for f in range(2):
                        ins = nc.tensor.matmul(psA[:, 64 + f:65 + f], inirow[0:1, f, :], ones[0:1, 0:1], start=True, stop=True)
                    ins.then_inc(ini_ps, 1)

                def own():
                    pe.wait_ge(own_ready, 1)
                    for q in range(BE // 512):
                        if q >= 2:
                            pe.wait_ge(own_free, q - 1)
                        nc.tensor.matmul((psA if q % 2 else psB)[0:BLOCKS, :], ksel[:, :], pre[:, q * 512:(q + 1) * 512],
                                         start=True, stop=True).then_inc(own_ps, 1)

                def group(j, last=False):
                    for i in range(GRP):
                        pe_transform_tile(nc, pe, j, i, last and i == GRP - 1, b)
                pe_transpose_tile(nc, pe, 0, 0, b)
                group(0)
                group(1)
                counts()
                group(2)
                group(3)
                own()
                with pe.Fori(4, GRP - 1) as j:
                    group(j)
                group(GRP - 1, True)
                pe.wait_ge(rel_ready, 1)
                n = 0
                for g in range(SG):
                    for f in range(4):
                        if n >= 2:
                            pe.wait_ge(col_free, n - 1)
                        from_ = relr[:, g, :] if f == 0 else srt[:, g, f * P:(f + 1) * P]
                        nc.tensor.transpose((psA if n % 2 else psB)[:, 0:P], from_, ident[:, :]).then_inc(col_ps, 1)
                        n += 1


def rgcn_gather(nc, kit, tag, iota, step_tab, yrow, tile_row, acc, y_tab):
    with ExitStack() as ctx:
        def sb(name, shape, dt=F32):
            return kit.sb(ctx, f"{tag}_{name}", shape, dt)

        def sem(name):
            return kit.sem(ctx, f"{tag}_{name}")

        rows = sb("rows", [P, 2, BS, D])
        idx = sb("idx", [P, 2, BS], U32)
        cols = sb("cols", [P, 2, BS, 2])
        onehot = sb("onehot", [P, 2, BS, P])
        ps = [kit.ps(ctx, f"{tag}_ps{s}") for s in range(BS)]
        rows_in = [sem("rows_in0"), sem("rows_in1")]
        idx_ready, cols_ready, onehot_ready, summed, added = sem("idx"), sem("cols"), sem("onehot"), sem("summed"), sem("added")
        pool_go = sem("pool_go")
        CREDIT = 2 * BS

        with nc.Block() as block:
            @block.gpsimd
            def _(pool):
                with pool.Fori(0, RG_BATCHES // 2) as j:
                    for h in range(2):
                        n = j * 2 + h
                        pool.wait_ge(summed, n * BS + BS)
                        pool.sem_inc(pool_go)
                        nc.gpsimd.tensor_copy(idx[:, h, :], yrow[:, bass.ds(n * BS, BS)]).then_inc(idx_ready, 1)
                        pool.wait_ge(idx_ready, n + 1)
                        pool.sem_inc(pool_go)
                        for s in range(BS):
                            nc.gpsimd.indirect_dma_start(rows[:, h, s, :], None, y_tab, bass.IndirectOffsetOnAxis(ap=idx[:, h, s:s + 1], axis=0)).then_inc(rows_in[h], 16)

            @block.vector
            def _(dve):
                def make_onehots_first(n, h):
                    nc.vector.tensor_copy(cols[:, h, :, :], step_tab[:, bass.ds(n * BS, BS), :]).then_inc(cols_ready, 1)

                def make_onehot(n, h, s):
                    nc.vector.tensor_scalar(onehot[:, h, s, :], iota[:, :], cols[:, h, s, 0:1], cols[:, h, s, 1:2],
                                            ALU.is_equal, ALU.mult).then_inc(onehot_ready, 1)

                dve.sem_inc(added, CREDIT)
                make_onehots_first(0, 0)
                dve.wait_ge(cols_ready, 1)
                for s in range(BS):
                    make_onehot(0, 0, s)
                with dve.Fori(0, RG_BATCHES // 2) as j:
                    for h in range(2):
                        n = j * 2 + h
                        dve.wait_ge(summed, n * BS + CREDIT)
                        make_onehots_first(n + 1, 1 - h)
                        dve.wait_ge(cols_ready, n + 2)
                        for s in range(BS):
                            make_onehot(n + 1, 1 - h, s)
                            tile = dve.value_load(tile_row[0:1, bass.ds(n * BS + s + BS, 1)], min_val=0, max_val=TILES - 1)
                            dve.wait_ge(summed, n * BS + s + 1 + CREDIT)
                            dve.wait_ge(added, n * BS + s + CREDIT)
                            to = acc[:, bass.ds(tile * D, D)]
                            nc.vector.tensor_tensor(to, to, ps[s][:, 0:D], ALU.add).then_inc(added, 1)

            @block.tensor
            def _(pe):
                pe.sem_inc(summed, CREDIT)
                with pe.Fori(0, RG_BATCHES // 2) as j:
                    for h in range(2):
                        n = j * 2 + h
                        pe.wait_ge(rows_in[h], (j + 1) * 16 * BS)
                        for s in range(BS):
                            pe.wait_ge(onehot_ready, n * BS + s + 1)
                            pe.wait_ge(added, n * BS + s + 1 + CREDIT - BS)
                            nc.tensor.matmul(ps[s][:, 0:D], onehot[:, h, s, :], rows[:, h, s, :], start=True, stop=True).then_inc(summed, 1)


def second_transform(nc, kit, comps, bases, roots, biases, ident, ones, acc, y_tab, key_tab, pen_tab):
    with ExitStack() as ctx:
        def sb(name, shape, dt=F32):
            return kit.sb(ctx, "s_" + name, shape, dt)

        def sem(name):
            return kit.sem(ctx, "s_" + name)

        b = Bag()
        b.W, b.root, b.bias = sb("W", [P, 2, R * D]), sb("root", [P, 2, D]), sb("bias", [1, D])
        b.src, b.hT, b.Y = sb("relu", [P, GRP, D]), sb("hT", [P, GRP, D]), sb("Y", [P, 4, 512])
        b.ident, b.ones, b.acc, b.y_tab = ident, ones, acc, y_tab
        basis, comp = sb("basis", [P, NB, 2, D]), sb("comp", [P, R * NB])
        keys, pen = sb("keys", [P, SG, P + 1]), sb("pen", [P, SG, P])
        b.psY = [kit.ps(ctx, f"s_psY{q}") for q in range(5)]
        b.psT = kit.ps(ctx, "s_psT")
        b.act_go, b.hT_ps, b.hT_sb, b.mm, b.evac = sem("act_go"), sem("hT_ps"), sem("hT_sb"), sem("mm"), sem("evac")
        b.stored = [sem("stored0"), sem("stored1")]
        relu_done, w_in, w_ready, dve_chain, keys_in, pen_ready, pen_out = (sem("relu_done"), sem("w_in"), sem("w_ready"), sem("dve"),
                                                                          sem("keys_in"), sem("pen_ready"), sem("pen_out"))

        def wait_src(pe, j, i):
            pe.wait_ge(relu_done, j * GRP + i + 1)

        def relu(t, i):
            nc.scalar.activation(b.src[:, i, :], acc[:, bass.ds(t * D, D)], ACT.Relu).then_inc(relu_done, 1)

        def refill(act, j, i):
            if not isinstance(j, int) or j * GRP + i + 2 < TILES:
                relu(j * GRP + i + 2, (i + 2) % GRP)
        b.wait_src, b.refill = wait_src, refill

        with nc.Block() as block:
            @block.sync
            def _(sp):
                load_weights(nc, sp, w_in, comps, bases, roots, biases, 1, basis, comp, b.root, b.bias)
                sp.dma_start(keys[:, :, :], flat_ap(key_tab, 0, [[P, P], [P * P, SG], [1, P + 1]])).then_inc(keys_in, 16)
                sp.wait_ge(pen_ready, 1)
                sp.dma_start(flat_ap(pen_tab, 0, [[P, P], [P * P, SG], [1, P]]), pen[:, :, :]).then_inc(pen_out, 16)
                sp.wait_ge(pen_out, 16)

            @block.vector
            def _(dve):
                link = chain(dve, dve_chain)
                dve.wait_ge(w_in, 64)
                mix_bases(nc, link, b.W, basis, comp)
                dve.wait_ge(keys_in, 16)
                nc.vector.tensor_tensor(pen[:, :, :], keys[:, :, 1:P + 1], keys[:, :, 0:P], ALU.is_equal).then_inc(w_ready, 1)
                dve.wait_ge(w_ready, 1)
                nc.vector.tensor_scalar(pen[:, :, :], pen[:, :, :], -1.0, BIG, ALU.add, ALU.mult).then_inc(pen_ready, 1)

            @block.scalar
            def _(act):
                relu(0, 0)
                relu(1, 1)
                act_transform(nc, act, b)

            @block.tensor
            def _(pe):
                pe.wait_ge(w_ready, 1)
                pe_transpose_tile(nc, pe, 0, 0, b)
                with pe.Fori(0, GRP - 1) as j:
                    for i in range(GRP):
                        pe_transform_tile(nc, pe, j, i, False, b)
                for i in range(GRP):
                    pe_transform_tile(nc, pe, GRP - 1, i, i == GRP - 1, b)


def project(nc, kit, x, gat_w, gat_as, gat_ad, ident, acc, adst, h_tab, xp_tab):
    with ExitStack() as ctx:
        def sb(name, shape, dt=F32):
            return kit.sb(ctx, "j_" + name, shape, dt)

        def sem(name):
            return kit.sem(ctx, "j_" + name)

        xin, y, h = sb("xin", [P, 2, GRP * D]), sb("y", [P, GRP * D]), sb("h", [P, 2, GRP * D])
        stats, mv, var, std, rstd = sb("stats", [P, GRP, 6]), sb("mv", [P, GRP, 2]), sb("var", [P, GRP]), sb("std", [P, GRP]), sb("rstd", [P, GRP])
        W, avec = sb("W", [P, 2, D]), sb("avec", [P, 2, D])
        hT, proj, prod, xp = sb("hT", [P, D]), sb("proj", [P, D]), sb("prod", [P, 2, D]), sb("xp", [P, GRP, XW])
        psT, psP = kit.ps(ctx, "j_psT"), kit.ps(ctx, "j_psP")
        w_in, x_in, tail_clear, y_ready, var_ready, std_ready, h_ready, h_out = (sem("w_in"), [sem("x_in0"), sem("x_in1")], sem("tail_clear"),
            sem("y_ready"), sem("var_ready"), sem("std_ready"), sem("h_ready"), [sem("h_out0"), sem("h_out1")])
        dve_c, hT_ps, hT_sb, proj_ps, proj_sb, xp_ready, xp_out = (sem("dve_c"), sem("hT_ps"), sem("hT_sb"), sem("proj_ps"), sem("proj_sb"),
                                                                 sem("xp_ready"), sem("xp_out"))
        with nc.Block() as block:
            @block.sync
            def _(sp):
                sp.dma_start(W[:, :, :], gat_w.rearrange("(k p) o -> p k o", p=P)).then_inc(w_in, 16)
                sp.dma_start(avec[:, 0, :], flat_ap(gat_as, 0, [[0, P], [1, D]])).then_inc(w_in, 16)
                sp.dma_start(avec[:, 1, :], flat_ap(gat_ad, 0, [[0, P], [1, D]])).then_inc(w_in, 16)
                sp.wait_ge(tail_clear, 1)
                def load_x(g):
                    full = GRP if g < GRP - 1 else GRP - 1
                    to = xin[:, g % 2, 0:full * D].rearrange("p (i c) -> p i c", c=D)
                    sp.dma_start(to, x[g * GRP * P:(g * GRP + full) * P, :].rearrange("(i p) c -> p i c", p=P)).then_inc(x_in[g % 2], 16)
                    if g == GRP - 1:
                        sp.dma_start(xin[0:LAST, g % 2, full * D:GRP * D], x[(TILES - 1) * P:N, :]).then_inc(x_in[g % 2], 16)
                load_x(0)
                load_x(1)
                for g in range(GRP):
                    sp.wait_ge(h_ready, g + 1)
                    sp.dma_start(h_tab[g * GRP * P:(g + 1) * GRP * P, :].rearrange("(i p) c -> p i c", p=P),
                                 h[:, g % 2, :].rearrange("p (i c) -> p i c", c=D)).then_inc(h_out[g % 2], 16)
                    if g + 2 < GRP:
                        sp.wait_ge(y_ready, g + 1)
                        load_x(g + 2)
                    sp.wait_ge(xp_ready, (g + 1) * GRP)
                    sp.dma_start(xp_tab[g * GRP * P:(g + 1) * GRP * P, :].rearrange("(i p) c -> p i c", p=P), xp[:, :, :]).then_inc(xp_out, 16)
                for k in range(2):
                    sp.wait_ge(h_out[k], 16 * ((GRP + 1 - k) // 2))
                sp.wait_ge(xp_out, 16 * GRP)

            @block.vector
            def _(dve):
                link = chain(dve, dve_c)
                v = nc.vector
                link(v.memset(xin[:, :, :], 0.0))
                v.memset(xp[:, :, :], 1.0).then_inc(tail_clear, 1)
                dve.wait_ge(w_in, 48)
                for g in range(GRP):
                    dve.wait_ge(x_in[g % 2], 16 * (g // 2 + 1) + (16 if g == GRP - 1 else 0))
                    v.tensor_tensor(y[:, :], xin[:, g % 2, :], acc[:, g * GRP * D:(g + 1) * GRP * D], ALU.add).then_inc(y_ready, 1)
                    dve.wait_ge(y_ready, g + 1)
                    for i in range(GRP):
                        ins = v.bn_stats(stats[:, i, :], y[:, i * D:(i + 1) * D])
                    link(ins)
                    for i in range(GRP):
                        ins = v.bn_aggr(mv[:, i, :], stats[:, i, :])
                    link(ins)
                    v.tensor_scalar(var[:, :], mv[:, :, 1], EPS, None, ALU.add).then_inc(var_ready, 1)
                    dve.wait_ge(std_ready, g + 1)
                    link(v.reciprocal(rstd[:, :], std[:, :]))
                    if g >= 2:
                        dve.wait_ge(h_out[g % 2], 16 * (g // 2))
                    for i in range(GRP):
                        ins = v.tensor_scalar(h[:, g % 2, i * D:(i + 1) * D], y[:, i * D:(i + 1) * D], mv[:, i, 0:1], rstd[:, i:i + 1],
                                              ALU.subtract, ALU.mult)
                    ins.then_inc(h_ready, 1)
                    for i in range(GRP):
                        t = g * GRP + i
                        dve.wait_ge(proj_sb, t + 1)
                        for k in range(2):
                            ins = v.tensor_tensor(prod[:, k, :], proj[:, :], avec[:, k, :], ALU.mult)
                        link(ins)
                        if g and i == 0:
                            dve.wait_ge(xp_out, 16 * g)
                        v.tensor_copy(xp[:, i, 0:GW].rearrange("p (h w) -> p h w", w=AW)[:, :, 0:OC], proj[:, :].rearrange("p (h w) -> p h w", w=OC))
                        v.tensor_reduce(xp[:, i, GW:XW], prod[:, 0, :].rearrange("p (h w) -> p h w", w=OC), AX.X, ALU.add)
                        link(v.tensor_reduce(adst[:, t * HD:(t + 1) * HD], prod[:, 1, :].rearrange("p (h w) -> p h w", w=OC), AX.X, ALU.add))
                        v.memset(var[:, 0:1], 0.0).then_inc(xp_ready, 1)

            @block.scalar
            def _(act):
                for g in range(GRP):
                    act.wait_ge(var_ready, g + 1)
                    nc.scalar.activation(std[:, :], var[:, :], ACT.Sqrt).then_inc(std_ready, 1)
                    for i in range(GRP):
                        t = g * GRP + i
                        act.wait_ge(hT_ps, t + 1)
                        nc.scalar.activation(hT[:, :], psT[:, 0:D], ACT.Copy).then_inc(hT_sb, 1)
                        act.wait_ge(proj_ps, t + 1)
                        if t:
                            act.wait_ge(xp_ready, t)
                        nc.scalar.activation(proj[:, :], psP[:, 0:D], ACT.Copy).then_inc(proj_sb, 1)

            @block.tensor
            def _(pe):
                pe.wait_ge(w_in, 48)
                for g in range(GRP):
                    pe.wait_ge(h_ready, g + 1)
                    for i in range(GRP):
                        t = g * GRP + i
                        for k in range(2):
                            ins = nc.tensor.transpose(psT[:, k * P:(k + 1) * P], h[:, g % 2, i * D + k * P:i * D + (k + 1) * P], ident[:, :])
                        ins.then_inc(hT_ps, 1)
                        pe.wait_ge(hT_sb, t + 1)
                        if t:
                            pe.wait_ge(proj_sb, t)
                        for k in range(2):
                            ins = nc.tensor.matmul(psP[:, 0:D], hT[:, k * P:(k + 1) * P], W[:, k, :], start=(k == 0), stop=(k == 1))
                        ins.then_inc(proj_ps, 1)


def gat_gather(nc, kit, ident, ones, iota, step_tab, srow, tile_row, acc, adst, xp_tab, pen_tab):
    with ExitStack() as ctx:
        def sb(name, shape, dt=F32):
            return kit.sb(ctx, "g_" + name, shape, dt)

        def sem(name):
            return kit.sem(ctx, "g_" + name)

        RING = 3
        BE_ = BS * P
        rows = sb("rows", [P, RING, BS, XW])
        idx = sb("idx", [P, RING, BS], U32)
        onehot = sb("onehot", [P, RING, BS, P])
        onehotT = sb("onehotT", [P, RING, BS, P])
        absd = sb("absd", [P, BS, P])
        ndst = sb("ndst", [P, BS])
        weighted = sb("weighted", [P, BS, GW])
        pen = sb("pen", [HD, RING, BE_ + 1])
        e = sb("e", [P, BS * HD])
        fwd = sb("fwd", [HD, BE_])
        mx = sb("mx", [HD, BE_])
        carry, going = sb("carry", [HD, 1]), sb("going", [HD, 1])
        drop, fac, facd = sb("drop", [HD, 1]), sb("fac", [HD, 1]), sb("facd", [HD, HD])
        expo, w, resc = sb("expo", [P, BS * HD]), sb("w", [P, BS * HD]), sb("resc", [P, HD])

        psS = [kit.ps(ctx, f"g_psS{i}") for i in range(2)]
        psE = kit.ps(ctx, "g_psE")
        psX = [kit.ps(ctx, f"g_psX{i}") for i in range(2)]
        psM = kit.ps(ctx, "g_psM")
        psO = [kit.ps(ctx, f"g_psO{i}") for i in range(2)]

        rows_in = [sem(f"rows_in{h}") for h in range(RING)]
        pen_in = [sem(f"pen_in{h}") for h in range(RING)]
        idx_ready, pool_go, ndst_ready, abs_ready, onehot_ready = sem("idx"), sem("pool_go"), sem("ndst"), sem("abs"), sem("onehot")
        sT_ps, sT_sb, ad_ps, e_ready, eT_ps = sem("sT_ps"), sem("sT_sb"), sem("ad_ps"), sem("e"), sem("eT_ps")
        fwd_ready, max_ready, drop_ready, fac_ready, facd_ready = sem("fwd"), sem("max"), sem("drop"), sem("fac_r"), sem("facd_r")
        fac_ps, expo_ready, w_ready, weighted_ready = sem("fac_ps"), sem("expo"), sem("w"), sem("weighted")
        summed, added, small, cleared = sem("summed"), sem("added"), sem("small"), sem("cleared")
        resc_ready, rescaled, act_go = sem("resc_r"), sem("rescaled"), sem("act_go")
        CREDIT = 2 * BS

        def tile_of(eng, step):
            return eng.value_load(tile_row[0:1, bass.ds(step + BS, 1)], min_val=0, max_val=TILES - 1)

        with nc.Block() as block:
            @block.gpsimd
            def _(pool):
                def gather(n, h, wait):
                    if wait is not None:
                        pool.wait_ge(weighted_ready, wait)
                        pool.sem_inc(pool_go)
                    nc.gpsimd.tensor_copy(idx[:, h, :], srow[:, bass.ds(n * BS, BS)]).then_inc(idx_ready, 1)
                    pool.wait_ge(idx_ready, n + 1)
                    pool.sem_inc(pool_go)
                    for s in range(BS):
                        nc.gpsimd.indirect_dma_start(rows[:, h, s, :], None, xp_tab,
                                                     bass.IndirectOffsetOnAxis(ap=idx[:, h, s:s + 1], axis=0)).then_inc(rows_in[h], 16)
                for n in range(RING):
                    gather(n, n, None)
                with pool.Fori(1, GAT_BATCHES // RING) as j:
                    for h in range(RING):
                        gather(j * RING + h, h, (j - 1) * RING + h + 1)
                gather(GAT_BATCHES, 0, GAT_BATCHES - RING + 1)
                pool.wait_ge(rows_in[0], (GAT_BATCHES // RING + 1) * 16 * BS)

            @block.sync
            def _(sp):
                def load(n, h, wait):
                    if wait is not None:
                        sp.wait_ge(drop_ready, wait)
                    sp.dma_start(pen[:, h, :], pen_tab[0:1, bass.ds(n * BE_, BE_ + 1)].to_broadcast([HD, BE_ + 1])).then_inc(pen_in[h], 16)
                for n in range(RING):
                    load(n, n, None)
                with sp.Fori(1, GAT_BATCHES // RING) as j:
                    for h in range(RING):
                        load(j * RING + h, h, (j - 1) * RING + h + 1)

            @block.scalar
            def _(act):
                def make_onehots(n, h, again):
                    if again:
                        act.wait_ge(onehot_ready, n)
                        act.sem_inc(act_go, 1)
                    nc.scalar.activation(ndst[:, :], step_tab[:, bass.ds(n * BS, BS), 0], ACT.Copy, scale=-1.0).then_inc(ndst_ready, 1)
                    act.wait_ge(ndst_ready, n + 1)
                    for s in range(BS):
                        ins = nc.scalar.activation(absd[:, s, :], iota[:, :], ACT.Abs, bias=ndst[:, s:s + 1])
                    ins.then_inc(abs_ready, 1)
                    act.wait_ge(abs_ready, n + 1)
                    nc.scalar.activation(onehot[:, h, :, :], absd[:, :, :], ACT.Relu, bias=ones[:, 0:1], scale=-1.0).then_inc(onehot_ready, 1)

                def copy_onehotsT(n, h):
                    for q in range(2):
                        act.wait_ge(sT_ps, 2 * n + q + 1)
                        nc.scalar.activation(onehotT[:, h, q * 4:q * 4 + 4, :], psS[q][:, :].rearrange("p (s e) -> p s e", e=P),
                                             ACT.Copy).then_inc(sT_sb, 1)

                make_onehots(0, 0, False)
                copy_onehotsT(0, 0)
                with act.Fori(0, GAT_BATCHES // RING) as j:
                    for h in range(RING):
                        n = j * RING + h
                        act.wait_ge(summed, (n - 1) * BS + CREDIT)
                        make_onehots(n + 1, (h + 1) % RING, True)
                        copy_onehotsT(n + 1, (h + 1) % RING)
                        act.wait_ge(drop_ready, n + 1)
                        nc.scalar.activation(fac[:, :], drop[:, :], ACT.Exp).then_inc(fac_ready, 1)
                        act.wait_ge(expo_ready, n + 1)
                        nc.scalar.activation(w[:, :], expo[:, :], ACT.Exp).then_inc(w_ready, 1)

            @block.tensor
            def _(pe):
                def transpose_onehots(n, h):
                    pe.wait_ge(onehot_ready, n + 1)
                    for q in range(2):
                        for s in range(4):
                            ins = nc.tensor.transpose(psS[q][:, s * P:(s + 1) * P], onehot[:, h, q * 4 + s, :], ident[:, :])
                        ins.then_inc(sT_ps, 1)

                def edge_logits(n, h):
                    for s in range(BS):
                        tile = tile_of(pe, n * BS + s)
                        if s % 4 == 0:
                            pe.wait_ge(sT_sb, 2 * n + s // 4 + 1)
                        ins = nc.tensor.matmul(psE[:, s * HD:(s + 1) * HD], onehotT[:, h, s, :], adst[:, bass.ds(tile * HD, HD)], start=True, stop=True)
                    ins.then_inc(ad_ps, 1)
                    pe.wait_ge(e_ready, n + 1)
                    for s in range(BS):
                        ins = nc.tensor.transpose(psX[s // 4][0:HD, s % 4 * P:(s % 4 + 1) * P], e[:, s * HD:(s + 1) * HD], ident[:, :])
                    ins.then_inc(eT_ps, 1)

                def sums(n, h):
                    pe.wait_ge(weighted_ready, n + 1)
                    for s in range(BS):
                        pe.wait_ge(added, n * BS + s - 1 + CREDIT)
                        nc.tensor.matmul(psO[s % 2][:, 0:GW], onehot[:, h, s, :], weighted[:, s, :], start=True, stop=True).then_inc(summed, 1)

                def turn(j, h, first):
                    n = j * RING + h
                    transpose_onehots(n + 1, (h + 1) % RING)
                    if not first:
                        sums(n - 1, (h + 2) % RING)
                    pe.wait_ge(max_ready, n + 1)
                    for s in range(BS):
                        nc.tensor.matmul(psM[:, s * HD:(s + 1) * HD], mx[:, s * P:(s + 1) * P], ident[0:HD, 0:HD], start=True, stop=True)
                    pe.wait_ge(facd_ready, n + 1)
                    nc.tensor.matmul(psM[:, BS * HD:(BS + 1) * HD], ones[0:HD, :], facd[:, :], start=True, stop=True).then_inc(fac_ps, 1)
                    edge_logits(n + 1, (h + 1) % RING)

                pe.sem_inc(summed, CREDIT)
                transpose_onehots(0, 0)
                edge_logits(0, 0)
                for h in range(RING):
                    turn(0, h, h == 0)
                with pe.Fori(1, GAT_BATCHES // RING) as j:
                    for h in range(RING):
                        turn(j, h, False)
                sums(GAT_BATCHES - 1, (GAT_BATCHES - 1) % RING)

            @block.vector
            def _(dve):
                v = nc.vector
                link = chain(dve, cleared)

                def add_logits(j, h):
                    n = j * RING + h
                    dve.wait_ge(rows_in[h], (j + 1) * 16 * BS)
                    dve.wait_ge(ad_ps, n + 1)
                    v.tensor_tensor(e[:, :].rearrange("p (s k) -> p s k", k=HD), rows[:, h, :, GW:XW],
                                    psE[:, 0:BS * HD].rearrange("p (s k) -> p s k", k=HD), ALU.add).then_inc(e_ready, 1)

                def adds(n):
                    for s in range(BS):
                        tile = tile_of(dve, n * BS + s)
                        if s == 0:
                            dve.wait_ge(rescaled, n + 1)
                        dve.wait_ge(summed, n * BS + s + 1 + CREDIT)
                        dve.wait_ge(added, n * BS + s + CREDIT)
                        to = acc[:, bass.ds(tile * GW, GW)]
                        v.tensor_tensor(to, to, psO[s % 2][:, 0:GW], ALU.add).then_inc(added, 1)

                def turn(j, h, first):
                    n = j * RING + h
                    dve.wait_ge(eT_ps, n + 1)
                    dve.wait_ge(pen_in[h], 16 * (j + 1))
                    dve.wait_ge(small, 3 * n + 1)
                    v.tensor_tensor_scan(fwd[:, 0:BE_ // 2], pen[:, h, 0:BE_ // 2], psX[0][0:HD, :], carry[:, :], ALU.add, ALU.max).then_inc(fwd_ready, 1)
                    dve.wait_ge(fwd_ready, 2 * n + 1)
                    v.tensor_tensor_scan(fwd[:, BE_ // 2:BE_], pen[:, h, BE_ // 2:BE_], psX[1][0:HD, :], fwd[:, BE_ // 2 - 1:BE_ // 2], ALU.add, ALU.max).then_inc(fwd_ready, 1)
                    dve.wait_ge(fwd_ready, 2 * n + 2)
                    v.tensor_tensor_scan(mx[:, ::-1], pen[:, h, 1:BE_ + 1][:, ::-1], fwd[:, ::-1], -BIG, ALU.add, ALU.max).then_inc(max_ready, 1)
                    v.tensor_scalar(going[:, :], pen[:, h, 0:1], 1.0 / BIG, 1.0, ALU.mult, ALU.add).then_inc(small, 1)
                    dve.wait_ge(max_ready, n + 1)
                    v.tensor_tensor(drop[:, :], carry[:, :], mx[:, 0:1], ALU.subtract).then_inc(small, 1)
                    dve.wait_ge(small, 3 * n + 3)
                    v.tensor_tensor(drop[:, :], drop[:, :], going[:, :], ALU.mult).then_inc(drop_ready, 1)
                    v.tensor_copy(carry[:, :], fwd[:, BE_ - 1:BE_]).then_inc(small, 1)
                    dve.wait_ge(fac_ready, n + 1)
                    v.scalar_tensor_tensor(out=facd[:, :], in0=ident[0:HD, 0:HD], scalar=fac[:, :], in1=ident[0:HD, 0:HD],
                                           op0=ALU.mult, op1=ALU.subtract).then_inc(facd_ready, 1)
                    if not first:
                        adds(n - 1)
                    dve.wait_ge(fac_ps, n + 1)
                    v.tensor_tensor(expo[:, :], e[:, :], psM[:, 0:BS * HD], ALU.subtract).then_inc(expo_ready, 1)
                    v.tensor_scalar(resc[:, :], psM[:, BS * HD:(BS + 1) * HD], onehotT[:, h, 0, 0:1], 1.0, ALU.mult, ALU.add).then_inc(resc_ready, 1)
                    tile = tile_of(dve, n * BS)
                    dve.wait_ge(resc_ready, n + 1)
                    dve.wait_ge(added, n * BS + CREDIT)
                    to = acc[:, bass.ds(tile * GW, GW)].rearrange("p (k w) -> p k w", w=AW)
                    v.tensor_tensor(to, to, resc[:, :].unsqueeze(2).to_broadcast([P, HD, AW]), ALU.mult).then_inc(rescaled, 1)
                    dve.wait_ge(expo_ready, n + 1)
                    add_logits(j + (h + 1) // RING, (h + 1) % RING)
                    dve.wait_ge(w_ready, n + 1)
                    v.tensor_tensor(weighted[:, :, :].rearrange("p s (k w) -> p s k w", w=AW),
                                    rows[:, h, :, 0:GW].rearrange("p s (k w) -> p s k w", w=AW),
                                    w[:, :].rearrange("p (s k) -> p s k", k=HD).unsqueeze(3).to_broadcast([P, BS, HD, AW]), ALU.mult).then_inc(weighted_ready, 1)

                link(v.memset(acc[:, :], 0.0))
                v.memset(carry[:, :], 0.0).then_inc(small, 1)
                dve.sem_inc(added, CREDIT)
                add_logits(0, 0)
                for h in range(RING):
                    turn(0, h, h == 0)
                with dve.Fori(1, GAT_BATCHES // RING) as j:
                    for h in range(RING):
                        turn(j, h, False)
                adds(GAT_BATCHES - 1)


def finish(nc, kit, acc, h_tab, out):
    with ExitStack() as ctx:
        def sb(name, shape, dt=F32):
            return kit.sb(ctx, "f_" + name, shape, dt)

        def sem(name):
            return kit.sem(ctx, "f_" + name)

        hin, y, o = sb("hin", [P, 2, GRP * D]), sb("y", [P, GRP * D]), sb("o", [P, 2, GRP * D])
        den = sb("den", [P, GRP * HD])
        stats, mv, var, std, rstd = sb("stats", [P, GRP, 6]), sb("mv", [P, GRP, 2]), sb("var", [P, GRP]), sb("std", [P, GRP]), sb("rstd", [P, GRP])
        h_in, y_ready, var_ready, std_ready, o_ready, chain_sem = [sem("h_in0"), sem("h_in1")], sem("y_ready"), sem("var_ready"), sem("std_ready"), sem("o_ready"), sem("chain")
        out_done = [sem("out0"), sem("out1")]
        with nc.Block() as block:
            @block.sync
            def _(sp):
                for g in range(GRP):
                    if g >= 2:
                        sp.wait_ge(y_ready, g - 1)
                    sp.dma_start(hin[:, g % 2, :].rearrange("p (i c) -> p i c", c=D),
                                 h_tab[g * GRP * P:(g + 1) * GRP * P, :].rearrange("(i p) c -> p i c", p=P)).then_inc(h_in[g % 2], 16)

            @block.gpsimd
            def _(pool):
                for g in range(GRP):
                    full = GRP if g < GRP - 1 else GRP - 1
                    pool.wait_ge(o_ready, g + 1)
                    pool.dma_start(out[g * GRP * P:(g * GRP + full) * P, :].rearrange("(i p) c -> p i c", p=P),
                                   o[:, g % 2, 0:full * D].rearrange("p (i c) -> p i c", c=D)).then_inc(out_done[g % 2], 16)
                pool.dma_start(out[(TILES - 1) * P:N, :], o[0:LAST, (GRP - 1) % 2, (GRP - 1) * D:GRP * D]).then_inc(out_done[(GRP - 1) % 2], 16)
                pool.wait_ge(out_done[0], 16 * 5)
                pool.wait_ge(out_done[1], 16 * 3)

            @block.scalar
            def _(act):
                for g in range(GRP):
                    act.wait_ge(var_ready, g + 1)
                    nc.scalar.activation(std[:, :], var[:, :], ACT.Sqrt).then_inc(std_ready, 1)

            @block.vector
            def _(dve):
                link = chain(dve, chain_sem)
                v = nc.vector
                for g in range(GRP):
                    a = acc[:, g * GRP * GW:(g + 1) * GRP * GW].rearrange("p (k w) -> p k w", w=AW)
                    yv = y[:, :].rearrange("p (k w) -> p k w", w=OC)
                    link(v.tensor_scalar(den[:, :], a[:, :, OC], 1e-16, None, ALU.add))
                    link(v.reciprocal(den[:, :], den[:, :]))
                    link(v.tensor_tensor(yv, a[:, :, 0:OC], den[:, :].unsqueeze(2).to_broadcast([P, GRP * HD, OC]), ALU.mult))
                    dve.wait_ge(h_in[g % 2], 16 * (g // 2 + 1))
                    v.tensor_tensor(y[:, :], y[:, :], hin[:, g % 2, :], ALU.add).then_inc(y_ready, 1)
                    dve.wait_ge(y_ready, g + 1)
                    for i in range(GRP):
                        ins = v.bn_stats(stats[:, i, :], y[:, i * D:(i + 1) * D])
                    link(ins)
                    for i in range(GRP):
                        ins = v.bn_aggr(mv[:, i, :], stats[:, i, :])
                    link(ins)
                    v.tensor_scalar(var[:, :], mv[:, :, 1], EPS, None, ALU.add).then_inc(var_ready, 1)
                    dve.wait_ge(std_ready, g + 1)
                    link(v.reciprocal(rstd[:, :], std[:, :]))
                    if g >= 2:
                        dve.wait_ge(out_done[g % 2], 16 * (g // 2))
                    for i in range(GRP):
                        ins = v.tensor_scalar(o[:, g % 2, i * D:(i + 1) * D], y[:, i * D:(i + 1) * D], mv[:, i, 0:1], rstd[:, i:i + 1],
                                              ALU.subtract, ALU.mult)
                    ins.then_inc(o_ready, 1)


_INS = ["x", "src", "dst", "edge_type_8", "L0_gnn_comps", "L0_gnn_bases", "L0_gnn_roots", "L0_gnn_biases",
        "L1_gnn_W", "L1_gnn_a_src", "L1_gnn_a_dst"]


def kernel(**inputs):
    import numpy as _np
    import concourse.bacc as _bacc
    from concourse import mybir as _mybir
    from concourse.bass_utils import run_bass_kernel_spmd as _run

    nc = _bacc.Bacc("TRN2", target_bir_lowering=False, num_devices=1)
    arrays, args = {}, []
    for name in _INS:
        a = _np.ascontiguousarray(inputs[name])
        arrays[f"in_{name}"] = a
        args.append(nc.dram_tensor(f"in_{name}", a.shape, _mybir.dt.from_np(a.dtype), kind="ExternalInput").ap())
    out = nc.dram_tensor("out_0", (N, D), F32, kind="ExternalOutput").ap()
    build(nc, *args, out)
    r = _run(nc, [arrays], core_ids=[0])
    return r.results[0]["out_0"]
```
